# Optimizing a Trainium2 kernel written in Bass

```python
import numpy as np
import jax
import jax.numpy as jnp

def _softmax(x, axis=-1):
    return jax.nn.softmax(x, axis=axis)

def _gelu(x):
    return jax.nn.gelu(x, approximate=True)

def _silu(x):
    return jax.nn.silu(x)

def _sigmoid(x):
    return jax.nn.sigmoid(x)

def _layernorm(x, axis=-1, eps=1e-05):
    m = jnp.mean(x, axis=axis, keepdims=True)
    v = jnp.var(x, axis=axis, keepdims=True)
    return (x - m) / jnp.sqrt(v + eps)

def _scatter_add(tgt, idx, src, axis=0):
    return tgt.at[idx].add(src)

def _segment_sum(src, seg, n):
    return jax.ops.segment_sum(src, seg, n)
kernel_name = 'mk_perceiver_d1_seqx_r2_fffc05'

def setup_inputs(seed: int=0):
    np.random.seed(seed)
    _w = jnp.asarray

    def _rec_inputs():
        import jax
        import jax.numpy as jnp
        _rk = jax.random.key(seed)
        x = -7.109e-05 + 0.9999 * jax.random.normal(jax.random.fold_in(_rk, 1), (8, 64, 2048), jnp.float32)
        _lenS = 64 - jax.random.randint(jax.random.fold_in(_rk, 7), (8,), 0, max(1, 64 // 4) + 1, jnp.int32)
        _lenS2 = 1601 - jax.random.randint(jax.random.fold_in(_rk, 8), (8,), 0, max(1, 1601 // 4) + 1, jnp.int32)
        _ctx_4096P = jax.random.normal(jax.random.fold_in(_rk, 11), (8, 16, 2048), jnp.float32)
        _ctx_4096c = jax.random.dirichlet(jax.random.fold_in(_rk, 511), 0.3 * jnp.ones((16,), jnp.float32), (8, 1601))
        _ctx_4096t = jnp.einsum('bsk,bkd->bsd', _ctx_4096c, _ctx_4096P)
        _ctx_4096t = _ctx_4096t * jax.lax.rsqrt(jnp.mean(jnp.square(_ctx_4096t)) + 1e-12) * 0.953939
        ctx_4096 = -0.00010331 + 0.999899 * (_ctx_4096t + 0.3 * jax.random.normal(jax.random.fold_in(_rk, 611), (8, 1601, 2048), jnp.float32))
        return (x, ctx_4096)
    x, ctx_4096 = _rec_inputs()

    def _L0_xattn_setup():
        import jax, jax.numpy as jnp
        import numpy as np
        key = jax.random.key(seed)
        k1, k2 = jax.random.split(key)
        B, Lq, Lk, D = (16, 512, 1024, 2048)
        query = jax.random.normal(k1, (B, Lq, D), dtype=jnp.float32)
        key_t = jax.random.normal(k2, (B, Lk, D), dtype=jnp.float32)
        return {'query': query, 'key': key_t}
    _L0_xattn_all = _L0_xattn_setup()
    _L0_xattn_in = {k: v for k, v in _L0_xattn_all.items() if k in ()}
    del _L0_xattn_all

    def _L0_attn_setup():
        import jax, jax.numpy as jnp
        import numpy as np
        NUM_HEADS = 32
        NUM_KV_HEADS = 8
        HEAD_DIM = 128
        key = jax.random.key(seed)
        ks = jax.random.split(key, 5)
        B, S, H = (2, 1024, 2048)
        Dq = NUM_HEADS * HEAD_DIM
        Dkv = NUM_KV_HEADS * HEAD_DIM
        return {'hidden_states': jax.random.normal(ks[0], (B, S, H), jnp.float32), 'w_q': jax.random.normal(ks[1], (H, Dq), jnp.float32) * 0.02, 'w_k': jax.random.normal(ks[2], (H, Dkv), jnp.float32) * 0.02, 'w_v': jax.random.normal(ks[3], (H, Dkv), jnp.float32) * 0.02, 'w_o': jax.random.normal(ks[4], (Dq, H), jnp.float32) * 0.02}
    _L0_attn_all = _L0_attn_setup()
    _L0_attn_in = {k: v for k, v in _L0_attn_all.items() if k in ('w_q', 'w_k', 'w_v', 'w_o')}
    del _L0_attn_all

    def _L0_ffn_setup():
        import jax, jax.numpy as jnp
        import numpy as np
        IN_F = 2048
        OUT_F = 2048
        RANK = 8
        NUM_EXPERTS = 64
        TOP_K = 16
        ROUTER_DIM = 16
        ALPHA = 32
        SCALING = ALPHA / TOP_K
        BOTTLENECK = NUM_EXPERTS * RANK
        key = jax.random.key(seed)
        ks = jax.random.split(key, 5)
        x = jax.random.normal(ks[0], (4, 2048, IN_F), dtype=jnp.float32)
        bound_a = float(np.sqrt(6.0 / IN_F))
        A_w = jax.random.uniform(ks[1], (BOTTLENECK, IN_F), jnp.float32, -bound_a, bound_a)
        B_w = jax.random.normal(ks[2], (OUT_F, BOTTLENECK), dtype=jnp.float32) * 0.02
        Wq_w = jax.random.normal(ks[3], (ROUTER_DIM, IN_F), dtype=jnp.float32) * 0.02
        keys = jax.random.normal(ks[4], (NUM_EXPERTS, ROUTER_DIM), dtype=jnp.float32) * 0.01
        return {'x': x, 'A_w': A_w, 'B_w': B_w, 'Wq_w': Wq_w, 'keys': keys}
    _L0_ffn_all = _L0_ffn_setup()
    _L0_ffn_in = {k: v for k, v in _L0_ffn_all.items() if k in ('A_w', 'B_w', 'Wq_w', 'keys')}
    del _L0_ffn_all
    return {'x': x, 'ctx_4096': ctx_4096, 'L0_attn_w_q': _L0_attn_in['w_q'], 'L0_attn_w_k': _L0_attn_in['w_k'], 'L0_attn_w_v': _L0_attn_in['w_v'], 'L0_attn_w_o': _L0_attn_in['w_o'], 'L0_ffn_A_w': _L0_ffn_in['A_w'], 'L0_ffn_B_w': _L0_ffn_in['B_w'], 'L0_ffn_Wq_w': _L0_ffn_in['Wq_w'], 'L0_ffn_keys': _L0_ffn_in['keys']}

def reference(x, ctx_4096, L0_attn_w_q, L0_attn_w_k, L0_attn_w_v, L0_attn_w_o, L0_ffn_A_w, L0_ffn_B_w, L0_ffn_Wq_w, L0_ffn_keys):
    import jax
    import jax.numpy as jnp

    def _L0_xattn_ref(query, key):
        import jax, jax.numpy as jnp
        import numpy as np
        a = jnp.einsum('bqd,bkd->bqk', query, key)
        e = jax.nn.softmax(a, axis=-1)
        c = jnp.einsum('bqk,bkd->bqd', e, key)
        return c

    def _L0_attn_ref(hidden_states, w_q, w_k, w_v, w_o):
        import jax, jax.numpy as jnp
        import numpy as np
        NUM_HEADS = 32
        NUM_KV_HEADS = 8
        HEAD_DIM = 128
        B, S, _ = hidden_states.shape
        Hq, Hkv, D = (NUM_HEADS, NUM_KV_HEADS, HEAD_DIM)
        g = Hq // Hkv
        scale = D ** (-0.5)
        q = (hidden_states @ w_q).reshape(B, S, Hkv, g, D)
        k = (hidden_states @ w_k).reshape(B, S, Hkv, D)
        v = (hidden_states @ w_v).reshape(B, S, Hkv, D)
        scores = jnp.einsum('bqhgd,bkhd->bhgqk', q, k) * scale
        causal = jnp.tril(jnp.ones((S, S), dtype=bool))
        scores = jnp.where(causal, scores, -jnp.inf)
        probs = jax.nn.softmax(scores.astype(jnp.float32), axis=-1).astype(q.dtype)
        attn = jnp.einsum('bhgqk,bkhd->bqhgd', probs, v)
        attn = attn.reshape(B, S, Hq * D)
        return attn @ w_o

    def _L0_ffn_ref(x, A_w, B_w, Wq_w, keys):
        import jax, jax.numpy as jnp
        import numpy as np
        IN_F = 2048
        OUT_F = 2048
        RANK = 8
        NUM_EXPERTS = 64
        TOP_K = 16
        ROUTER_DIM = 16
        ALPHA = 32
        SCALING = ALPHA / TOP_K
        BOTTLENECK = NUM_EXPERTS * RANK
        q = jnp.einsum('bsd,rd->bsr', x, Wq_w)
        scores = jnp.einsum('bsr,er->bse', q, keys)
        top_vals, top_idx = jax.lax.top_k(scores, TOP_K)
        top_w = jax.nn.softmax(top_vals, axis=-1)
        gate = jnp.sum(jax.nn.one_hot(top_idx, NUM_EXPERTS, dtype=top_w.dtype) * top_w[..., None], axis=-2)
        z = jnp.einsum('bsd,nd->bsn', x, A_w)
        z = z.reshape(*z.shape[:-1], NUM_EXPERTS, RANK)
        z_gated = (z * gate[..., None]).reshape(*z.shape[:-2], BOTTLENECK)
        out = jnp.einsum('bsn,on->bso', z_gated, B_w) * SCALING
        return out
    x = x + _L0_xattn_ref(_layernorm(x, axis=-1), ctx_4096)
    x = x + _L0_attn_ref(_layernorm(x, axis=-1), L0_attn_w_q, L0_attn_w_k, L0_attn_w_v, L0_attn_w_o)
    x = x + _L0_ffn_ref(_layernorm(x, axis=-1), L0_ffn_A_w, L0_ffn_B_w, L0_ffn_Wq_w, L0_ffn_keys)
    return x

_drawn_inputs = setup_inputs


def setup_inputs(seed=0):
    import zlib

    import numpy as np

    out = dict(_drawn_inputs(seed))
    spreads = {}
    factors = {}
    for name, (base, spread) in spreads.items():
        noise = np.random.default_rng([zlib.crc32(name.encode()), seed]).standard_normal(out[name].shape)
        drawn = base * np.exp(spread * noise) if base else spread * noise
        out[name] = jnp.asarray(drawn.astype(out[name].dtype))
    for name, factor in factors.items():
        out[name] = (out[name] * factor).astype(out[name].dtype)
    return out
```

```python
import concourse.bass as bass
from concourse import mybir
from contextlib import ExitStack

F32 = mybir.dt.float32
F32R = mybir.dt.float32r
I32 = mybir.dt.int32
ALU = mybir.AluOpType
ACT = mybir.ActivationFunctionType
AX = mybir.AxisListType

P = 128
B, LQ, D = 8, 64, 2048
LK = 1601
DC = D // P
NCOL = D // 512
EPS = 1e-5

ROWS = B * LQ
RT = ROWS // P

NBLK = 3
KT = 4
BLK = KT * P
TAIL = LK - NBLK * BLK
TPAD = TAIL + TAIL % 2
TQ = 4
PIECES = NBLK * NCOL
LAG = 2
NAT = 4


def transposes():
    base = [("q", 0), ("q", 1)] + [("c", 0, c) for c in range(DC)] + [("t", k) for k in range(DC // TQ)]
    base += [("c", 1, c) for c in range(DC)] + [("c", 2, c) for c in range(DC)]
    base.insert(5, ("e", 2))
    base.insert(29, ("e", 0))
    base.insert(46, ("e", 1))
    return base


TRANS = transposes()
NT = len(TRANS)
E2_AT = TRANS.index(("e", 2))
SCORE_STEPS = DC + DC // TQ + (NBLK - 1) * DC
SCORES_END = [DC + DC // TQ, 2 * DC + DC // TQ, SCORE_STEPS]

UNITS = [(j, c, k) for j in range(NBLK) for c in range(NCOL) for k in range(KT + (j == 0))]
NU = len(UNITS)
FIRST_OF = [UNITS.index((j, 0, 0)) for j in range(NBLK)] + [NU]
LAST_OF = {(j, c): max(u for u, v in enumerate(UNITS) if v[:2] == (j, c)) for j in range(NBLK) for c in range(NCOL)}
C1_NOW = 6


def unit_slots():
    at = [[] for _ in range(NT)]

    def spread(units, prev, lo, hi):
        for n, u in enumerate(units):
            at[lo + n * (hi - lo) // len(units)].append((u, prev))

    spread(range(FIRST_OF[1] + C1_NOW, FIRST_OF[2]), True, 2, 12)
    spread(range(FIRST_OF[2], NU), True, 12, 29)
    spread(range(0, FIRST_OF[1]), False, 31, 51)
    spread(range(FIRST_OF[1], FIRST_OF[1] + C1_NOW), False, 51, NT)
    return at


UNITS_AT = unit_slots()
NATURAL_AT = [[] for _ in range(NT)]
for _s, _us in enumerate(UNITS_AT):
    NATURAL_AT[max(_s - 2, 0)] += _us
HALF_AT, STATS_AT, EXP_AT = {25: 0, 42: 1, 0: 2}, {26: 0, 43: 1, 1: 2}, {27: 0, 44: 1, 2: 2}
SUM_AT, FOLD_AT, FINISH_AT = 4, 30, 31
STATS_OF_X_AT, NORM_AT = (45, 47, 48, 49), 51


def kernel_program(nc, x, ctx, w_q, w_k, w_v, w_o, a_w, b_w, wq_w, keys, out):
    x1 = nc.dram_tensor("x1_scratch", (ROWS, D), F32, kind="Internal").ap()
    cross_attention(nc, x.rearrange("b q d -> (b q) d"), ctx, x1)
    with (nc.sbuf_tensor("rows", [P, RT, D], F32) as rows,
          nc.sbuf_tensor("h_hi", [P, DC, ROWS], F32R) as h_hi,
          nc.sbuf_tensor("h_lo", [P, DC, ROWS], F32R) as h_lo,
          nc.sbuf_tensor("row_bn", [P, RT, NCOL, 6], F32) as row_bn,
          nc.sbuf_tensor("ident", [P, P], F32) as ident):
        self_attention(nc, x1, w_q, w_k, w_v, w_o, rows, h_hi, h_lo, row_bn, ident)
        feed_forward(nc, a_w, b_w, wq_w, keys, rows, h_hi, h_lo, row_bn, ident, out.rearrange("b q d -> (b q) d"))


def make_identity(nc, pool, ident, sem):
    pool.memset(ident[:], 0.0).then_inc(sem, 1)
    pool.wait_ge(sem, 1)
    pool.affine_select(out=ident[:], in_=ident[:], compare_op=ALU.not_equal, fill=1.0, base=0,
                       pattern=[[-1, P]], channel_multiplier=1).then_inc(sem, 1)


def rsqrt_steps(link, dve, w, var):
    link(dve.tensor_scalar(w[:, 1:2], var, EPS, None, ALU.add))
    link(dve.tensor_scalar(w[:, 2:3], w[:, 1:2], -0.5, None, ALU.mult))
    link(dve.tensor_scalar(w[:, 3:4].bitcast(I32), w[:, 1:2].bitcast(I32), 1, None, ALU.logical_shift_right))
    link(dve.tensor_scalar(w[:, 0:1].bitcast(I32), w[:, 3:4].bitcast(I32), -1, 0x5f3759df, ALU.mult, ALU.add))
    for _ in range(4):
        link(dve.tensor_scalar(w[:, 3:4], w[:, 0:1], w[:, 0:1], w[:, 2:3], ALU.mult, ALU.mult))
        link(dve.scalar_tensor_tensor(out=w[:, 0:1], in0=w[:, 3:4], scalar=1.5, in1=w[:, 0:1],
                                      op0=ALU.add, op1=ALU.mult))


RSQRT_LINKS = 12


def cross_attention(nc, x_rows, ctx, x1):
    ctx_v = ctx[:, 0:NBLK * BLK, :].rearrange("b (j k p) (c n) -> b j c p k n", k=KT, p=P, n=512)
    stack = ExitStack()
    with stack:
        def sb(name, shape, dt=F32):
            return stack.enter_context(nc.sbuf_tensor(name, shape, dt))

        def ps(name, shape):
            return stack.enter_context(nc.psum_tensor(name, shape, F32))

        def sem(name):
            return stack.enter_context(nc.semaphore(name))

        ident = sb("xa_ident", [P, P])
        raw = sb("xa_raw", [P, PIECES, KT, 512])
        raw_tail = sb("xa_raw_tail", [P, D])
        nat_hi = sb("xa_nat_hi", [P, NAT, 512], F32R)
        nat_lo = sb("xa_nat_lo", [P, NAT, 512], F32R)
        ct_hi = sb("xa_ct_hi", [P, 3, 512], F32R)
        ct_lo = sb("xa_ct_lo", [P, 3, 512], F32R)
        q_t = sb("xa_q_t", [P, DC, 2 * LQ], F32R)
        e_t = sb("xa_e_t", [P, NBLK, KT + 1, 2 * LQ], F32R)
        xq = sb("xa_xq", [LQ, D])
        xr = sb("xa_xr", [LQ, D])
        acc = sb("xa_acc", [P, D])
        fold = sb("xa_fold", [LQ, D])
        res = sb("xa_res", [LQ, D])
        half = sb("xa_half", [LQ, BLK + TAIL])
        scores = sb("xa_scores", [LQ, BLK + TAIL])
        expo = sb("xa_expo", [LQ, BLK + TAIL])
        mx = sb("xa_mx", [LQ, NBLK])
        run_max = sb("xa_run_max", [LQ, NBLK])
        neg_max = sb("xa_neg_max", [LQ, NBLK])
        row_sum = sb("xa_row_sum", [LQ, NBLK])
        alpha = sb("xa_alpha", [P, NBLK])
        total = sb("xa_total", [LQ, 3])
        bn = sb("xa_bn", [LQ, NCOL, 6])
        mv = sb("xa_mv", [LQ, 2])
        rs_w = sb("xa_rs_w", [LQ, 4])

        ps_t = ps("xa_ps_t", [P, 3, 512])
        ps_s = ps("xa_ps_s", [P, 3, 512])
        ps_o = ps("xa_ps_o", [P, 2, 512])
        s_bank = [0, 2, 1]
        s_len = [BLK + TAIL, BLK, BLK]

        ident_ready = sem("xa_ident_ready")
        pad_ready = sem("xa_pad_ready")
        raw_in = [sem(f"xa_raw_in{n}") for n in range(PIECES)]
        tail_in = sem("xa_tail_in")
        xq_in = sem("xa_xq_in")
        xr_in = sem("xa_xr_in")
        q_ready = sem("xa_q_ready")
        t_done = sem("xa_t_done")
        hi_done = sem("xa_hi_done")
        lo_done = sem("xa_lo_done")
        s_done = sem("xa_s_done")
        pv_done = sem("xa_pv_done")
        nat_act = sem("xa_nat_act")
        nat_pool = sem("xa_nat_pool")
        nat_dve = sem("xa_nat_dve")
        half_ready = sem("xa_half_ready")
        stats_ready = sem("xa_stats_ready")
        e_ready = sem("xa_e_ready")
        alpha_ready = sem("xa_alpha_ready")
        acc_done = sem("xa_acc_done")
        folded = sem("xa_folded")
        res_ready = sem("xa_res_ready")
        stored = sem("xa_stored")
        chain = sem("xa_chain")

        def t_index(b, at):
            return NT * b + at - (0 if isinstance(b, int) and b == 0 and at < E2_AT else 1)

        def t_bank(b, at):
            return (at - (0 if isinstance(b, int) and b == 0 and at < E2_AT else 1)) % 3

        def present(b, at):
            if isinstance(b, int) and b == 0:
                return at != E2_AT
            return not (isinstance(b, int) and b == B) or at == E2_AT

        def e_slot(b, at):
            return (t_index(b, 0), 2) if isinstance(b, int) and b == B else (t_index(b, at), t_bank(b, at))

        def units(b, at, table):
            for u, prev in table[at]:
                if prev and not (isinstance(b, int) and b == 0):
                    yield b - 1, u
                elif not prev and not (isinstance(b, int) and b == B):
                    yield b, u

        def owner(b, j, at_map, at):
            if j == 2:
                return None if isinstance(b, int) and b == 0 else b - 1
            return None if isinstance(b, int) and b == B else b

        def shared(u):
            return u % NAT == 3

        def split_count(u):
            return u // NAT * 3 + u % NAT + 1

        PER_SHARED, PER_DVE = NU // NAT * 3, NU // NAT

        def turns(eng, body):
            body(0)
            with eng.Fori(1, B - 1) as b:
                body(b)
            body(B - 1)
            body(B)

        def natural(j, c, k):
            if k == KT:
                return raw_tail[0:TAIL, c * 512:(c + 1) * 512], TAIL
            return raw[:, j * NCOL + c, k, :], P

        def score_rows(p0, j):
            flat = ps_s[p0:p0 + LQ, :, :].rearrange("p a n -> p (a n)")
            return flat[:, s_bank[j] * 512:s_bank[j] * 512 + s_len[j]]

        def links_per_turn():
            own = sum(shared(u) for u in range(NU))
            return own + (2 + 3 + 3) + 3 + 1 + (1 + 1 + RSQRT_LINKS)

        block = stack.enter_context(nc.Block())

        @block.sync
        def _(sp):
            def load_piece(b, j, c):
                sp.dma_start(raw[:, j * NCOL + c, :, :], ctx_v[b, j, c]).then_inc(raw_in[j * NCOL + c], 16)

            def load_tail(b):
                sp.dma_start(raw_tail[0:TAIL, :], ctx[b, NBLK * BLK:LK, :]).then_inc(tail_in, 16)

            def load_rows(b, dst, s):
                sp.dma_start(dst[:], x_rows[bass.ds(b * LQ, LQ), :]).then_inc(s, 16)

            load_rows(0, xq, xq_in)
            sp.wait_ge(pad_ready, 1)
            for c in range(NCOL):
                load_piece(0, 0, c)
            load_tail(0)
            for j in (1, 2):
                for c in range(NCOL):
                    load_piece(0, j, c)

            def turn(b):
                first = isinstance(b, int) and b == 0
                end = isinstance(b, int) and b == B
                last = isinstance(b, int) and b == B - 1
                if not end and not last:
                    sp.wait_ge(t_done, t_index(b, 1) + 1)
                    load_rows(b + 1, xq, xq_in)
                if not first:
                    if not end:
                        for j in (1, 2):
                            for c in range(NCOL):
                                sp.wait_ge(pv_done, NU * (b - 1) + LAST_OF[j, c] + 1)
                                load_piece(b, j, c)
                    sp.wait_ge(res_ready, b)
                    sp.dma_start(x1[bass.ds((b - 1) * LQ, LQ), :], res[:]).then_inc(stored, 16)
                if not end:
                    if not first:
                        sp.wait_ge(stored, 16 * b)
                    load_rows(b, xr, xr_in)
                    if not last:
                        for c in range(NCOL):
                            sp.wait_ge(pv_done, NU * b + LAST_OF[0, c] + 1)
                            load_piece(b + 1, 0, c)
                        load_tail(b + 1)

            turns(sp, turn)
            sp.wait_ge(stored, 16 * B)

        @block.gpsimd
        def _(pool):
            make_identity(nc, pool, ident, ident_ready)
            pool.wait_ge(ident_ready, 2)
            pool.memset(raw_tail[64:P, :], 0.0).then_inc(pad_ready, 1)

            def turn(b):
                for at in range(NT):
                    for bb, u in units(b, at, NATURAL_AT):
                        if shared(u):
                            continue
                        j, c, k = UNITS[u]
                        src, rows = natural(j, c, k)
                        pool.wait_ge(nat_act, PER_SHARED * bb + split_count(u))
                        pool.tensor_tensor(nat_lo[0:rows, u % NAT, :], src, nat_hi[0:rows, u % NAT, :].bitcast(F32),
                                           ALU.subtract).then_inc(nat_pool, 1)

            turns(pool, turn)

        @block.scalar
        def _(act):
            def evacuate(b, at):
                what = TRANS[at]
                n, bank = e_slot(b, at)
                act.wait_ge(t_done, n + 1)
                if what[0] == "q":
                    h = what[1]
                    act.activation(q_t[:, 8 * h:8 * h + 8, 0:LQ], ps_t[:, bank, :].rearrange("p (c q) -> p c q", q=LQ),
                                   ACT.Copy).then_inc(hi_done, 1)
                elif what[0] == "e":
                    j = what[1]
                    src = ps_t[:, bank, :].rearrange("p (c q) -> p c q", q=LQ)
                    if j == 0:
                        act.activation(e_t[0:TAIL, j, KT, 0:LQ], src[0:TAIL, KT, :], ACT.Copy)
                    act.activation(e_t[:, j, 0:KT, 0:LQ], src[:, 0:KT, :], ACT.Copy).then_inc(hi_done, 1)
                else:
                    w = 512 if what[0] == "c" else TQ * TPAD
                    act.activation(ct_hi[:, bank, 0:w], ps_t[:, bank, 0:w], ACT.Copy).then_inc(hi_done, 1)

            def turn(b):
                for at in range(NT):
                    if at in HALF_AT:
                        j = HALF_AT[at]
                        o = owner(b, j, HALF_AT, at)
                        if o is not None:
                            act.wait_ge(s_done, SCORE_STEPS * o + SCORES_END[j])
                            act.activation(half[:, 0:s_len[j]], score_rows(64, j), ACT.Copy).then_inc(half_ready, 1)
                    if present(b, at):
                        evacuate(b, at)
                    for bb, u in units(b, at, NATURAL_AT):
                        if shared(u):
                            continue
                        j, c, k = UNITS[u]
                        src, rows = natural(j, c, k)
                        if not (isinstance(bb, int) and bb == 0 and u < NAT):
                            act.wait_ge(pv_done, NU * bb + u - NAT + 1)
                        act.activation(nat_hi[0:rows, u % NAT, :], src, ACT.Copy).then_inc(nat_act, 1)
                    if at in EXP_AT:
                        j = EXP_AT[at]
                        o = owner(b, j, EXP_AT, at)
                        if o is not None:
                            act.wait_ge(stats_ready, NBLK * o + j + 1)
                            act.activation(expo[:, 0:s_len[j]], scores[:, 0:s_len[j]], ACT.Exp,
                                           bias=neg_max[:, j:j + 1], accum_out=row_sum[:, j:j + 1]).then_inc(e_ready, 1)
                            if j:
                                act.activation(alpha[0:LQ, j:j + 1], run_max[:, j - 1:j], ACT.Exp,
                                               bias=neg_max[:, j:j + 1]).then_inc(alpha_ready, 1)
                                act.wait_ge(alpha_ready, 2 * (NBLK - 1) * o + 2 * j - 1)
                                act.activation(alpha[LQ:P, j:j + 1], alpha[0:LQ, j:j + 1], ACT.Copy).then_inc(alpha_ready, 1)
                    if at == FOLD_AT and not (isinstance(b, int) and b == 0):
                        act.wait_ge(acc_done, PIECES * b)
                        act.activation(fold[:], acc[LQ:P, :], ACT.Copy).then_inc(folded, 1)

            turns(act, turn)

        @block.vector
        def _(dve):
            links = {"n": 0, "base": 0}

            def link(ins):
                ins.then_inc(chain, 1)
                links["n"] += 1
                dve.wait_ge(chain, links["base"] + links["n"])

            def layernorm_rows():
                link(dve.bn_aggr(mv[:], bn[:]))
                rsqrt_steps(link, dve, rs_w, mv[:, 1:2])
                dve.tensor_scalar(xq[:], xq[:], mv[:, 0:1], rs_w[:, 0:1], ALU.subtract, ALU.mult).then_inc(q_ready, 1)

            def row_stats(c):
                i = dve.bn_stats(bn[:, c, :], xq[:, c * 512:(c + 1) * 512])
                if c == NCOL - 1:
                    link(i)

            dve.wait_ge(xq_in, 16)
            for c in range(NCOL):
                row_stats(c)
            layernorm_rows()

            def evacuate(b, at):
                what = TRANS[at]
                n, bank = e_slot(b, at)
                dve.wait_ge(hi_done, n + 1)
                if what[0] == "q":
                    h = what[1]
                    dve.tensor_tensor(q_t[:, 8 * h:8 * h + 8, LQ:2 * LQ], ps_t[:, bank, :].rearrange("p (c q) -> p c q", q=LQ),
                                      q_t[:, 8 * h:8 * h + 8, 0:LQ].bitcast(F32), ALU.subtract).then_inc(lo_done, 1)
                elif what[0] == "e":
                    j = what[1]
                    src = ps_t[:, bank, :].rearrange("p (c q) -> p c q", q=LQ)
                    if j == 0:
                        dve.tensor_tensor(e_t[0:TAIL, j, KT, LQ:2 * LQ], src[0:TAIL, KT, :],
                                          e_t[0:TAIL, j, KT, 0:LQ].bitcast(F32), ALU.subtract)
                    dve.tensor_tensor(e_t[:, j, 0:KT, LQ:2 * LQ], src[:, 0:KT, :],
                                      e_t[:, j, 0:KT, 0:LQ].bitcast(F32), ALU.subtract).then_inc(lo_done, 1)
                else:
                    w = 512 if what[0] == "c" else TQ * TPAD
                    dve.tensor_tensor(ct_lo[:, bank, 0:w], ps_t[:, bank, 0:w], ct_hi[:, bank, 0:w].bitcast(F32),
                                      ALU.subtract).then_inc(lo_done, 1)

            def block_stats(o, j):
                n = s_len[j]
                dve.wait_ge(half_ready, NBLK * o + j + 1)
                if not (isinstance(o, int) and o == 0 and j == 0):
                    dve.wait_ge(e_ready, NBLK * o + j)
                link(dve.tensor_tensor(scores[:, 0:n], score_rows(0, j), half[:, 0:n], ALU.add))
                dst = run_max if j == 0 else mx
                link(dve.tensor_reduce(dst[:, j:j + 1], scores[:, 0:n], AX.X, ALU.max))
                if j:
                    link(dve.tensor_tensor(run_max[:, j:j + 1], run_max[:, j - 1:j], mx[:, j:j + 1], ALU.max))
                dve.tensor_scalar(neg_max[:, j:j + 1], run_max[:, j:j + 1], -1.0, None, ALU.mult).then_inc(stats_ready, 1)

            def row_total(o):
                dve.wait_ge(e_ready, NBLK * (o + 1))
                dve.wait_ge(alpha_ready, 2 * (NBLK - 1) * (o + 1))
                link(dve.tensor_scalar(total[:, 0:1], row_sum[:, 0:1], alpha[0:LQ, 1:2], row_sum[:, 1:2], ALU.mult, ALU.add))
                link(dve.tensor_scalar(total[:, 1:2], total[:, 0:1], alpha[0:LQ, 2:3], row_sum[:, 2:3], ALU.mult, ALU.add))
                link(dve.reciprocal(total[:, 2:3], total[:, 1:2]))

            def accumulate(bb, j, c):
                d = j * NCOL + c
                col = slice(c * 512, (c + 1) * 512)
                dve.wait_ge(pv_done, NU * bb + LAST_OF[j, c] + 1)
                if j == 0:
                    dve.tensor_copy(acc[:, col], ps_o[:, d % 2, :]).then_inc(acc_done, 1)
                else:
                    dve.wait_ge(alpha_ready, 2 * (NBLK - 1) * bb + 2 * j)
                    dve.wait_ge(acc_done, PIECES * bb + d - NCOL + 1)
                    dve.scalar_tensor_tensor(out=acc[:, col], in0=acc[:, col], scalar=alpha[:, j:j + 1],
                                             in1=ps_o[:, d % 2, :], op0=ALU.mult, op1=ALU.add).then_inc(acc_done, 1)

            def turn(b):
                first = isinstance(b, int) and b == 0
                end = isinstance(b, int) and b == B
                last = isinstance(b, int) and b == B - 1
                due = []
                for at in range(NT):
                    if present(b, at):
                        evacuate(b, at)
                    if at in STATS_AT:
                        j = STATS_AT[at]
                        o = owner(b, j, STATS_AT, at)
                        if o is not None:
                            block_stats(o, j)
                    for bb, u in units(b, at, NATURAL_AT):
                        if not shared(u):
                            continue
                        j, c, k = UNITS[u]
                        src, rows = natural(j, c, k)
                        if not (isinstance(bb, int) and bb == 0 and u < NAT):
                            dve.wait_ge(pv_done, NU * bb + u - NAT + 1)
                        link(dve.tensor_copy(nat_hi[0:rows, u % NAT, :], src))
                        dve.tensor_tensor(nat_lo[0:rows, u % NAT, :], src, nat_hi[0:rows, u % NAT, :].bitcast(F32),
                                          ALU.subtract).then_inc(nat_dve, 1)
                    for bb, j, c in due:
                        accumulate(bb, j, c)
                    due = [(bb, *UNITS[u][:2]) for bb, u in units(b, at, UNITS_AT) if LAST_OF[UNITS[u][:2]] == u]
                    if at == SUM_AT and not first:
                        row_total(b - 1)
                    if at == FINISH_AT and not first:
                        dve.wait_ge(folded, b)
                        dve.wait_ge(xr_in, 16 * b)
                        dve.wait_ge(acc_done, PIECES * b)
                        link(dve.tensor_tensor(res[:], acc[0:LQ, :], fold[:], ALU.add))
                        dve.scalar_tensor_tensor(out=res[:], in0=res[:], scalar=total[:, 2:3], in1=xr[:],
                                                 op0=ALU.mult, op1=ALU.add).then_inc(res_ready, 1)
                    if not end and not last:
                        if at in STATS_OF_X_AT:
                            if at == STATS_OF_X_AT[0]:
                                dve.wait_ge(xq_in, 16 * (b + 2))
                            row_stats(STATS_OF_X_AT.index(at))
                        if at == NORM_AT:
                            layernorm_rows()
                for bb, j, c in due:
                    accumulate(bb, j, c)

            turn(0)
            before = links["n"]
            per_turn = links_per_turn()
            with dve.Fori(1, B - 1) as b:
                links["n"], links["base"] = 0, before + (b - 1) * per_turn
                turn(b)
                assert links["n"] == per_turn, (links["n"], per_turn)
            links["n"], links["base"] = 0, before + (B - 2) * per_turn
            turn(B - 1)
            turn(B)

        @block.tensor
        def _(pe):
            pe.wait_ge(ident_ready, 2)
            pe.wait_ge(q_ready, 1)

            def transpose_slot(b, at):
                what = TRANS[at]
                n, bank = e_slot(b, at)
                if what[0] in "ct" and not (isinstance(b, int) and b == 0 and n < 3):
                    pe.wait_ge(lo_done, n - 2)
                ins = []
                if what[0] == "q":
                    for c in range(8):
                        g = 8 * what[1] + c
                        ins.append(pe.transpose(ps_t[:, bank, c * LQ:(c + 1) * LQ], xq[:, g * P:(g + 1) * P], ident[0:LQ, 0:LQ]))
                elif what[0] == "c":
                    j, g = what[1:]
                    if g % KT == 0:
                        pe.wait_ge(raw_in[j * NCOL + g // KT], 16 * (b + 1))
                    for k in range(KT):
                        ins.append(pe.transpose(ps_t[:, bank, k * P:(k + 1) * P],
                                                raw[:, j * NCOL + g // KT, k, g % KT * P:(g % KT + 1) * P], ident[:]))
                elif what[0] == "t":
                    if what[1] == 0:
                        pe.wait_ge(tail_in, 16 * (b + 1))
                    for c in range(TQ):
                        g = TQ * what[1] + c
                        ins.append(pe.transpose(ps_t[:, bank, c * TPAD:(c + 1) * TPAD], raw_tail[0:TPAD, g * P:(g + 1) * P],
                                                ident[0:TPAD, 0:TPAD]))
                else:
                    j = what[1]
                    for k in range(KT):
                        ins.append(pe.transpose(ps_t[:, bank, k * LQ:(k + 1) * LQ], expo[:, k * P:(k + 1) * P], ident[0:LQ, 0:LQ]))
                    if j == 0:
                        ins.append(pe.transpose(ps_t[0:TAIL, bank, KT * LQ:(KT + 1) * LQ], expo[:, BLK:BLK + TAIL],
                                                ident[0:LQ, 0:LQ]))
                ins[-1].then_inc(t_done, 1)

            def score(b, at):
                what = TRANS[at]
                bank = t_bank(b, at)
                pe.wait_ge(lo_done, t_index(b, at) + 1)
                if what[0] == "c":
                    j, g = what[1:]
                    o = ps_s[:, s_bank[j], :]
                    pe.matmul(o, q_t[:, g, :], ct_hi[:, bank, :], start=g == 0, stop=False)
                    i = pe.matmul(o, q_t[:, g, :], ct_lo[:, bank, :], start=False, stop=g == DC - 1)
                else:
                    o = ps_s[:, s_bank[0] + 1, 0:TPAD]
                    for c in range(TQ):
                        g = TQ * what[1] + c
                        col = slice(c * TPAD, (c + 1) * TPAD)
                        pe.matmul(o, q_t[:, g, :], ct_hi[:, bank, col], start=g == 0, stop=False)
                        i = pe.matmul(o, q_t[:, g, :], ct_lo[:, bank, col], start=False, stop=g == DC - 1)
                i.then_inc(s_done, 1)

            def product(bb, u, e_at):
                j, c, k = UNITS[u]
                d = j * NCOL + c
                rows = TAIL if k == KT else P
                if shared(u):
                    pe.wait_ge(nat_dve, PER_DVE * bb + u // NAT + 1)
                else:
                    pe.wait_ge(nat_pool, PER_SHARED * bb + split_count(u))
                if u == FIRST_OF[j]:
                    pe.wait_ge(lo_done, e_at)
                if k == 0 and not (isinstance(bb, int) and bb == 0 and d < 2):
                    pe.wait_ge(acc_done, PIECES * bb + d - 1)
                o = ps_o[:, d % 2, :]
                pe.matmul(o, e_t[0:rows, j, k, :], nat_hi[0:rows, u % NAT, :], start=k == 0, stop=False)
                pe.matmul(o, e_t[0:rows, j, k, :], nat_lo[0:rows, u % NAT, :], start=False,
                          stop=u == LAST_OF[j, c]).then_inc(pv_done, 1)

            def turn(b):
                end = isinstance(b, int) and b == B
                for at in range(NT + LAG):
                    if at < NT and present(b, at):
                        transpose_slot(b, at)
                    if at + 1 < NT and TRANS[at + 1][0] == "e" and present(b, at + 1):
                        j = TRANS[at + 1][1]
                        pe.wait_ge(e_ready, NBLK * (b - 1 if j == 2 else b) + j + 1)
                    if at == NT + LAG - 1 and not end and not (isinstance(b, int) and b == B - 1):
                        pe.wait_ge(q_ready, b + 2)
                    if at >= LAG and TRANS[at - LAG][0] in "ct" and not end:
                        score(b, at - LAG)
                    if at < NT:
                        for bb, u in units(b, at, UNITS_AT):
                            j = UNITS[u][0]
                            e_at = e_slot(b, TRANS.index(("e", j)))[0] + 1 if u == FIRST_OF[j] else None
                            product(bb, u, e_at)

            turns(pe, turn)


def rows_norm_vector(dve, link, rows, bn, mv, w, normed, norm_ready, normed_free):
    for r in range(RT):
        i = dve.bn_aggr(mv[:, r, :], bn[:, r, :, :])
    link(i)
    link(dve.tensor_scalar(w[:, 1, :], mv[:, :, 1], EPS, None, ALU.add))
    link(dve.tensor_scalar(w[:, 2, :], w[:, 1, :], -0.5, None, ALU.mult))
    link(dve.tensor_scalar(w[:, 3, :].bitcast(I32), w[:, 1, :].bitcast(I32), 1, None, ALU.logical_shift_right))
    link(dve.tensor_scalar(w[:, 0, :].bitcast(I32), w[:, 3, :].bitcast(I32), -1, 0x5f3759df, ALU.mult, ALU.add))
    for _ in range(4):
        link(dve.tensor_tensor(w[:, 3, :], w[:, 0, :], w[:, 0, :], ALU.mult))
        link(dve.tensor_tensor(w[:, 3, :], w[:, 3, :], w[:, 2, :], ALU.mult))
        link(dve.scalar_tensor_tensor(out=w[:, 0, :], in0=w[:, 3, :], scalar=1.5, in1=w[:, 0, :],
                                      op0=ALU.add, op1=ALU.mult))
    for r in range(RT):
        normed_free(r)
        dve.tensor_scalar(normed[:, r % 2, :], rows[:, r, :], mv[:, r, 0:1], w[:, 0, r:r + 1],
                          ALU.subtract, ALU.mult).then_inc(norm_ready, 1)


QUADS = DC // 4
NORM_T = RT * QUADS


def rows_transpose_slot(pe, n, normed, ident, ps, bank):
    r, q = n // QUADS, n % QUADS
    for c in range(4):
        g = 4 * q + c
        i = pe.transpose(ps[:, bank, c * P:(c + 1) * P], normed[:, r % 2, g * P:(g + 1) * P], ident[:])
    return i


def h_slot(h, n):
    r, q = n // QUADS, n % QUADS
    return h[:, 4 * q:4 * q + 4, r * P:(r + 1) * P]


def quad(ps, bank):
    return ps[:, bank, :].rearrange("p (c n) -> p c n", n=P)


def three_products(pe, out, hi, lo, mov_hi, mov_lo, first, last):
    pe.matmul(out, hi, mov_hi, start=first, stop=False)
    pe.matmul(out, hi, mov_lo, start=False, stop=False)
    return pe.matmul(out, lo, mov_hi, start=False, stop=last)


GROUPS, HG, HD = 8, 4, 128
SCALE = HD ** -0.5
PROJ = ["k", "q0", "v", "q1", "q2", "q3"]
NP = len(PROJ)
NI = NP + NCOL
UNIT_SM = 2 * RT * 2


def self_attention(nc, x1, w_q, w_k, w_v, w_o, rows, h_hi, h_lo, row_bn, ident):
    stack = ExitStack()
    with stack:
        def sb(name, shape, dt=F32):
            return stack.enter_context(nc.sbuf_tensor(name, shape, dt))

        def sem(name):
            return stack.enter_context(nc.semaphore(name))

        raw = sb("sa_raw", [P, 2, D])
        w_hi = sb("sa_w_hi", [P, 2, D], F32R)
        w_lo = sb("sa_w_lo", [P, 2, D], F32R)
        normed = sb("sa_normed", [P, 2, D])
        mv = sb("sa_mv", [P, RT, 2])
        rs_w = sb("sa_rs_w", [P, 4, RT])
        k_t = sb("sa_k_t", [P, ROWS])
        q_t = sb("sa_q_t", [P, B, HG, LQ])
        v_t = sb("sa_v_t", [P, ROWS])
        v = sb("sa_v", [P, RT, HD])
        mask = sb("sa_mask", [P, LQ])
        s_sb = sb("sa_s", [P, UNIT_SM, LQ])
        prob = sb("sa_prob", [P, UNIT_SM, LQ])
        s_max = sb("sa_s_max", [P, UNIT_SM])
        s_sum = sb("sa_s_sum", [P, UNIT_SM])
        s_inv = sb("sa_s_inv", [P, UNIT_SM])
        p_t = sb("sa_p_t", [P, 2 * RT, P])
        o_hi = sb("sa_o_hi", [P, HG, ROWS], F32R)
        o_lo = sb("sa_o_lo", [P, HG, ROWS], F32R)

        ps_mm = stack.enter_context(nc.psum_tensor("sa_ps_mm", [P, 2, 512], F32))
        ps_s = stack.enter_context(nc.psum_tensor("sa_ps_s", [P, UNIT_SM, LQ], F32))
        ps_p = stack.enter_context(nc.psum_tensor("sa_ps_p", [P, 2 * RT, P], F32))
        ps_o = stack.enter_context(nc.psum_tensor("sa_ps_o", [P, 2, 512], F32))

        rows_in = [sem(f"sa_rows_in{r}") for r in range(RT)]
        ident_ready = sem("sa_ident_ready")
        mask_ready = sem("sa_mask_ready")
        norm_ready = sem("sa_norm_ready")
        nt_done = sem("sa_nt_done")
        nt_hi = sem("sa_nt_hi")
        nt_lo = sem("sa_nt_lo")
        w_in = [sem(f"sa_w_in{n}") for n in range(2)]
        w_hi_done = sem("sa_w_hi_done")
        w_lo_done = sem("sa_w_lo_done")
        proj_done = sem("sa_proj_done")
        proj_out = sem("sa_proj_out")
        wo_bank = sem("sa_wo_bank")
        wo_added = sem("sa_wo_added")
        s_done = sem("sa_s_done")
        s_shifted = sem("sa_s_shifted")
        exp_done = sem("sa_exp_done")
        prob_ready = sem("sa_prob_ready")
        pt_done = sem("sa_pt_done")
        pt_out = sem("sa_pt_out")
        pv_done = sem("sa_pv_done")
        o_hi_done = sem("sa_o_hi_done")
        o_lo_done = sem("sa_o_lo_done")
        vt_done = sem("sa_vt_done")
        v_out = sem("sa_v_out")
        chain = sem("sa_chain")

        def item0(g):
            return 0 if isinstance(g, int) and g == 0 else NP + NI * (g - 1)

        def kind(g):
            first, end = isinstance(g, int) and g == 0, isinstance(g, int) and g == GROUPS
            return (0 if end else NP), (0 if first else NCOL)

        def turns(eng, body):
            body(0)
            with eng.Fori(1, GROUPS) as g:
                body(g)
            body(GROUPS)

        def o_rows(o, half, b2):
            t = o[:, :, half * 2 * P:(half + 1) * 2 * P].rearrange("p h (r b q) -> p r h b q", r=2, b=2)
            return t[:, :, :, b2, :]

        def o_ps(b2):
            return ps_o[:, b2, :].rearrange("p (r h q) -> p r h q", r=2, h=HG)

        block = stack.enter_context(nc.Block())

        @block.sync
        def _(sp):
            for r in range(RT):
                sp.dma_start(rows[:, r, :], x1[r * P:(r + 1) * P, :]).then_inc(rows_in[r], 16)

            w_k_v = w_k.rearrange("(c p) n -> p c n", p=P)
            w_v_v = w_v.rearrange("(c p) n -> p c n", p=P)
            w_q_v = w_q.rearrange("(c p) n -> p c n", p=P)
            w_o_v = w_o.rearrange("(g h p) n -> g p h n", h=HG, p=P)

            def turn(g):
                n_proj, n_wo = kind(g)
                srcs = []
                for what in PROJ[:n_proj]:
                    if what == "k":
                        srcs.append(w_k_v[:, :, bass.ds(g * HD, HD)])
                    elif what == "v":
                        srcs.append(w_v_v[:, :, bass.ds(g * HD, HD)])
                    else:
                        srcs.append(w_q_v[:, :, bass.ds((g * HG + int(what[1])) * HD, HD)])
                for c in range(n_wo):
                    srcs.append(w_o_v[g - 1, :, :, c * 512:(c + 1) * 512])
                for n, src in enumerate(srcs):
                    if not (isinstance(g, int) and g == 0 and n < 2):
                        sp.wait_ge(w_lo_done, item0(g) + n - 1)
                    dst = raw[:, n % 2, :]
                    dst = dst.rearrange("p (c n) -> p c n", n=src.shape[-1])
                    sp.dma_start(dst, src).then_inc(w_in[n % 2], 16)

            turns(sp, turn)

        @block.gpsimd
        def _(pool):
            make_identity(nc, pool, ident, ident_ready)
            pool.wait_ge(ident_ready, 2)
            pool.memset(mask[:], 0.0).then_inc(mask_ready, 1)
            for a in range(2):
                pool.wait_ge(mask_ready, a + 1)
                half = mask[a * LQ:(a + 1) * LQ, :]
                pool.affine_select(out=half, in_=half, compare_op=ALU.is_ge, fill=-3.0e38, base=0,
                                   pattern=[[-1, LQ]], channel_multiplier=1).then_inc(mask_ready, 1)
            pool.wait_ge(mask_ready, 3)
            with pool.Fori(0, (NP + NI * (GROUPS - 1) + NCOL) // 2) as i:
                for n in range(2):
                    pool.wait_ge(w_hi_done, 2 * i + n + 1)
                    pool.tensor_tensor(w_lo[:, n, :], raw[:, n, :], w_hi[:, n, :].bitcast(F32),
                                       ALU.subtract).then_inc(w_lo_done, 1)

        @block.scalar
        def _(act):
            def split(g, n):
                act.wait_ge(w_in[n % 2], 8 * (item0(g) + n - n % 2) + 16)
                n_proj = kind(g)[0]
                if n >= 2 and n - 2 < n_proj:
                    act.wait_ge(proj_done, NP * g + n - 1)
                elif n >= 2:
                    act.wait_ge(wo_bank, NCOL * RT * (g - 1) + RT * (n - 1 - n_proj))
                act.activation(w_hi[:, n % 2, :], raw[:, n % 2, :], ACT.Copy).then_inc(w_hi_done, 1)

            split(0, 0)
            split(0, 1)
            for n in range(NORM_T):
                act.wait_ge(nt_done, n + 1)
                act.activation(h_slot(h_hi, n), quad(ps_mm, n % 2), ACT.Copy).then_inc(nt_hi, 1)

            def turn(g):
                n_proj, n_wo = kind(g)
                if n_wo:
                    act.wait_ge(s_shifted, g)
                    act.activation(prob[:], s_sb[:], ACT.Exp).then_inc(exp_done, 1)

                def probs_t():
                    act.wait_ge(pt_done, g)
                    act.activation(p_t[:], ps_p[:], ACT.Copy).then_inc(pt_out, 1)

                def heads_out(half):
                    for b2 in range(2):
                        act.wait_ge(pv_done, 4 * (g - 1) + 2 * half + b2 + 1)
                        act.activation(o_rows(o_hi, half, b2), o_ps(b2), ACT.Copy).then_inc(o_hi_done, 1)

                if n_wo and not n_proj:
                    probs_t()
                    heads_out(0)
                    heads_out(1)
                for n, what in enumerate(PROJ[:n_proj]):
                    act.wait_ge(proj_done, NP * g + n + 1)
                    dst = {"k": k_t, "v": v_t}.get(what)
                    dst = q_t[:, :, int(what[1]), :] if dst is None else dst[:].rearrange("p (b q) -> p b q", q=LQ)
                    act.activation(dst, ps_mm[:, n % 2, :].rearrange("p (b q) -> p b q", q=LQ), ACT.Copy).then_inc(proj_out, 1)
                    if n_wo and what == "k":
                        probs_t()
                    if n_wo and what == "q0":
                        heads_out(0)
                    if n_wo and what == "v":
                        heads_out(1)
                    if what == "q1":
                        act.wait_ge(vt_done, g + 1)
                        act.activation(v[:], quad(ps_o, 0), ACT.Copy).then_inc(v_out, 1)
                    split(g, n + 2)
                for c in range(n_wo if n_proj else 2):
                    split(g, n_proj + c + 2)

            turns(act, turn)

        @block.vector
        def _(dve):
            links = [0]

            def link(ins):
                ins.then_inc(chain, 1)
                links[0] += 1
                dve.wait_ge(chain, links[0])

            for r in range(RT):
                dve.wait_ge(rows_in[r], 16)
                for c in range(NCOL):
                    i = dve.bn_stats(row_bn[:, r, c, :], rows[:, r, c * 512:(c + 1) * 512])
            link(i)

            def normed_free(r):
                if r >= 2:
                    dve.wait_ge(nt_done, QUADS * (r - 1))

            def lo_parts(n):
                dve.wait_ge(nt_hi, n + 1)
                dve.tensor_tensor(h_slot(h_lo, n), quad(ps_mm, n % 2), h_slot(h_hi, n).bitcast(F32),
                                  ALU.subtract).then_inc(nt_lo, 1)

            def free_or_evacuate(r):
                if r >= 2:
                    for n in range((r - 2) * QUADS, (r - 1) * QUADS):
                        lo_parts(n)
                normed_free(r)

            rows_norm_vector(dve, link, rows, row_bn, mv, rs_w, normed, norm_ready, free_or_evacuate)
            for n in range(2 * QUADS, NORM_T):
                lo_parts(n)
            base = links[0]

            SOFTMAX_LINKS = 4
            dve.wait_ge(mask_ready, 3)

            def turn(g):
                n_proj, n_wo = kind(g)
                if not n_wo:
                    dve.memset(s_inv[:], 0.0).then_inc(wo_added, 1)
                    return
                last = isinstance(g, int) and g == GROUPS
                here = base + SOFTMAX_LINKS * (g - 1)

                def step(ins, n):
                    ins.then_inc(chain, 1)
                    dve.wait_ge(chain, here + n)

                dve.wait_ge(s_done, g)
                step(dve.scalar_tensor_tensor(out=s_sb[:], in0=ps_s[:], scalar=SCALE,
                                              in1=mask[:].unsqueeze(1).to_broadcast([P, UNIT_SM, LQ]),
                                              op0=ALU.mult, op1=ALU.add), 1)
                step(dve.tensor_reduce(s_max[:], s_sb[:], AX.X, ALU.max), 2)
                dve.tensor_tensor(s_sb[:], s_sb[:], s_max[:].unsqueeze(2).to_broadcast([P, UNIT_SM, LQ]),
                                  ALU.subtract).then_inc(s_shifted, 1)
                dve.wait_ge(exp_done, g)
                step(dve.tensor_reduce(s_sum[:], prob[:], AX.X, ALU.add), 3)
                step(dve.reciprocal(s_inv[:], s_sum[:]), 4)
                dve.tensor_tensor(prob[:], prob[:], s_inv[:].unsqueeze(2).to_broadcast([P, UNIT_SM, LQ]),
                                  ALU.mult).then_inc(prob_ready, 1)
                for half in range(2):
                    for b2 in range(2):
                        dve.wait_ge(o_hi_done, 4 * (g - 1) + 2 * half + b2 + 1)
                        dve.tensor_tensor(o_rows(o_lo, half, b2), o_ps(b2), o_rows(o_hi, half, b2).bitcast(F32),
                                          ALU.subtract).then_inc(o_lo_done, 1)
                for c in range(NCOL):
                    for r in range(RT):
                        n = RT * c + r
                        dve.wait_ge(wo_bank, NCOL * RT * (g - 1) + n + 1)
                        part = rows[:, r, c * 512:(c + 1) * 512]
                        dve.tensor_tensor(part, part, ps_mm[:, n % 2, :], ALU.add).then_inc(wo_added, 1)
                        if last:
                            dve.wait_ge(wo_added, 1 + NCOL * RT * (g - 1) + n + 1)
                            dve.bn_stats(row_bn[:, r, c, :], part)

            turns(dve, turn)

        @block.tensor
        def _(pe):
            pe.wait_ge(ident_ready, 2)
            for n in range(NORM_T):
                if n % QUADS == 0:
                    pe.wait_ge(norm_ready, n // QUADS + 1)
                if n >= 2:
                    pe.wait_ge(nt_lo, n - 1)
                rows_transpose_slot(pe, n, normed, ident, ps_mm, n % 2).then_inc(nt_done, 1)
            pe.wait_ge(nt_lo, NORM_T)

            def project(g, n):
                n0 = item0(g)
                pe.wait_ge(w_lo_done, n0 + n + 1)
                if n < 2 and not (isinstance(g, int) and g == 0):
                    pe.wait_ge(wo_added, 1 + NCOL * RT * (g - 1))
                elif n >= 2:
                    pe.wait_ge(proj_out, NP * g + n - 1)
                for c in range(DC):
                    col = slice(c * HD, (c + 1) * HD)
                    i = three_products(pe, ps_mm[:, n % 2, :], w_hi[:, n % 2, col], w_lo[:, n % 2, col],
                                       h_hi[:, c, :], h_lo[:, c, :], c == 0, c == DC - 1)
                i.then_inc(proj_done, 1)

            def attend_scores(g):
                pe.wait_ge(proj_out, NP * g)
                for r in range(RT):
                    for hp in range(2):
                        for b2 in range(2):
                            q0 = (2 * r + b2) * LQ
                            i = pe.matmul(ps_s[:, (2 * r + hp) * 2 + b2, :], q_t[:, 2 * r + b2, 2 * hp:2 * hp + 2, :],
                                          k_t[:, q0:q0 + LQ], start=True, stop=True)
                i.then_inc(s_done, 1)

            def probs_transpose(g):
                pe.wait_ge(prob_ready, g)
                for u in range(2 * RT):
                    i = pe.transpose(ps_p[:, u, :], prob[:, 2 * u:2 * u + 2, :], ident[:])
                i.then_inc(pt_done, 1)

            def attend_values(g, half):
                if half == 0:
                    pe.wait_ge(pt_out, g)
                    pe.wait_ge(v_out, g)
                else:
                    pe.wait_ge(o_lo_done, 4 * (g - 1) + 2)
                for b2 in range(2):
                    part = slice(b2 * LQ, (b2 + 1) * LQ)
                    for r2 in range(2):
                        r = 2 * half + r2
                        i = pe.matmul(ps_o[:, b2, r2 * 256:(r2 + 1) * 256], v[part, r, :], p_t[part, 2 * r:2 * r + 2, :],
                                      start=True, stop=True)
                    i.then_inc(pv_done, 1)

            def values_transpose(g):
                pe.wait_ge(proj_out, NP * g + PROJ.index("v") + 1)
                if not (isinstance(g, int) and g == 0):
                    pe.wait_ge(o_lo_done, 4 * g)
                for r in range(RT):
                    i = pe.transpose(ps_o[:, 0, r * P:(r + 1) * P], v_t[:, r * P:(r + 1) * P], ident[:])
                i.then_inc(vt_done, 1)

            def times_w_o(g, c):
                n0 = item0(g)
                n = kind(g)[0] + c
                pe.wait_ge(w_lo_done, n0 + n + 1)
                if c == 0:
                    pe.wait_ge(o_lo_done, 4 * g)
                    if not (isinstance(g, int) and g == GROUPS):
                        pe.wait_ge(proj_out, NP * (g + 1))
                for r in range(RT):
                    m = RT * c + r
                    if m >= 2:
                        pe.wait_ge(wo_added, 1 + NCOL * RT * (g - 1) + m - 1)
                    for h in range(HG):
                        col = slice(r * P, (r + 1) * P)
                        wc = slice(h * 512, (h + 1) * 512)
                        i = three_products(pe, ps_mm[:, m % 2, :], o_hi[:, h, col], o_lo[:, h, col],
                                           w_hi[:, n % 2, wc], w_lo[:, n % 2, wc], h == 0, h == HG - 1)
                    i.then_inc(wo_bank, 1)

            def turn(g):
                n_proj, n_wo = kind(g)
                if n_wo:
                    attend_scores(g)
                if n_proj:
                    project(g, 0)
                if n_wo:
                    probs_transpose(g)
                if n_proj:
                    project(g, 1)
                if n_wo:
                    attend_values(g, 0)
                if n_proj:
                    project(g, 2)
                if n_wo:
                    attend_values(g, 1)
                if n_proj:
                    project(g, 3)
                    values_transpose(g)
                    project(g, 4)
                    project(g, 5)
                if n_wo:
                    for c in range(NCOL):
                        times_w_o(g, c)

            turns(pe, turn)


EXPERTS, RANK, RD, TOP = 64, 8, 16, 16
NZ = EXPERTS * RANK
ZC = NZ // P
SCALING = 2.0
ITEMS = ZC + NCOL
WQ_LO = 32


def feed_forward(nc, a_w, b_w, wq_w, keys, rows, h_hi, h_lo, row_bn, ident, out_rows):
    stack = ExitStack()
    with stack:
        def sb(name, shape, dt=F32):
            return stack.enter_context(nc.sbuf_tensor(name, shape, dt))

        def sem(name):
            return stack.enter_context(nc.semaphore(name))

        raw = sb("ff_raw", [P, 2, D])
        w_hi = sb("ff_w_hi", [P, 2, D], F32R)
        w_lo = sb("ff_w_lo", [P, 2, D], F32R)
        normed = sb("ff_normed", [P, 2, D])
        mv = sb("ff_mv", [P, RT, 2])
        rs_w = sb("ff_rs_w", [P, 4, RT])
        wq_sb = sb("ff_wq", [RD, D])
        wq_t = sb("ff_wq_t", [P, DC, P], F32R)
        keys_sb = sb("ff_keys", [EXPERTS, RD])
        keys_t = sb("ff_keys_t", [RD, EXPERTS])
        sc = sb("ff_scores", [P, RT, EXPERTS])
        best = sb("ff_best", [P, RT, TOP])
        rest = sb("ff_rest", [P, 2, RT, EXPERTS])
        chosen = sb("ff_chosen", [P, RT, EXPERTS])
        shifted = sb("ff_shifted", [P, RT, EXPERTS])
        expo = sb("ff_expo", [P, RT, EXPERTS])
        gate = sb("ff_gate", [P, RT, EXPERTS])
        g_sum = sb("ff_g_sum", [P, RT])
        g_inv = sb("ff_g_inv", [P, RT])
        gate_t = sb("ff_gate_t", [EXPERTS, ROWS])
        expand = sb("ff_expand", [EXPERTS, ZC, P])
        gates = normed[:, 0, :].rearrange("p (a n) -> p a n", a=ZC)
        z = normed[:, 1, 0:2 * ROWS].rearrange("p (a n) -> p a n", a=2)
        q_half = normed[0:RD, 1, 2 * ROWS:3 * ROWS]
        q_t = normed[0:RD, 1, 3 * ROWS:4 * ROWS]
        z_hi = sb("ff_z_hi", [P, ZC, ROWS], F32R)
        z_lo = sb("ff_z_lo", [P, ZC, ROWS], F32R)

        ps_t = stack.enter_context(nc.psum_tensor("ff_ps_t", [P, 3, 512], F32))
        ps_mm = stack.enter_context(nc.psum_tensor("ff_ps_mm", [P, 2, 512], F32))
        ps_r = stack.enter_context(nc.psum_tensor("ff_ps_r", [P, 3, 512], F32))

        small_in = sem("ff_small_in")
        raw_in = [sem(f"ff_raw_in{n}") for n in range(2)]
        expand_ready = sem("ff_expand_ready")
        wq_zero = sem("ff_wq_zero")
        norm_ready = sem("ff_norm_ready")
        t_done = sem("ff_t_done")
        hi_done = sem("ff_hi_done")
        lo_done = sem("ff_lo_done")
        keys_out = sem("ff_keys_out")
        q_done = sem("ff_q_done")
        q_half_out = sem("ff_q_half_out")
        q_ready = sem("ff_q_ready")
        sc_done = sem("ff_sc_done")
        sc_shifted = sem("ff_sc_shifted")
        exp_done = sem("ff_exp_done")
        gate_ready = sem("ff_gate_ready")
        gt_done = sem("ff_gt_done")
        gt_out = sem("ff_gt_out")
        gx_done = sem("ff_gx_done")
        gx_out = sem("ff_gx_out")
        z_done = sem("ff_z_done")
        z_gated = sem("ff_z_gated")
        z_hi_done = sem("ff_z_hi_done")
        z_lo_done = sem("ff_z_lo_done")
        o_done = sem("ff_o_done")
        o_added = sem("ff_o_added")
        stored = sem("ff_stored")
        chain = sem("ff_chain")

        T_ITEM0, T_WQ, T_ITEMS = NORM_T, NORM_T + 4, NORM_T + 5

        def t_item(m, q):
            return T_ITEM0 + q if m == 0 else T_ITEMS + 4 * (m - 1) + q

        block = stack.enter_context(nc.Block())

        @block.sync
        def _(sp):
            sp.dma_start(wq_sb[:], wq_w).then_inc(small_in, 16)
            sp.dma_start(keys_sb[:], keys).then_inc(small_in, 16)
            b_v = b_w.rearrange("(b j p) n -> b p j n", j=4, p=P)
            for m in range(ITEMS):
                if m >= 2:
                    sp.wait_ge(t_done, t_item(m - 2, 3) + 1)
                if m < ZC:
                    sp.dma_start(raw[:, m % 2, :], a_w[m * P:(m + 1) * P, :]).then_inc(raw_in[m % 2], 16)
                else:
                    sp.dma_start(raw[:, m % 2, :].rearrange("p (j n) -> p j n", j=4), b_v[m - ZC]).then_inc(raw_in[m % 2], 16)
            for c in range(NCOL):
                for r in range(RT):
                    sp.wait_ge(o_added, RT * c + r + 1)
                    sp.dma_start(out_rows[r * P:(r + 1) * P, c * 512:(c + 1) * 512],
                                 rows[:, r, c * 512:(c + 1) * 512]).then_inc(stored, 16)
            sp.wait_ge(stored, 16 * NCOL * RT)

        @block.gpsimd
        def _(pool):
            pool.memset(wq_t[:].bitcast(F32), 0.0).then_inc(wq_zero, 1)
            pool.wait_ge(wq_zero, 1)
            pool.memset(expand[:], 0.0).then_inc(expand_ready, 1)
            pool.wait_ge(expand_ready, 1)
            v = expand[:].rearrange("e a (m r) -> e a m r", r=RANK)
            pool.affine_select(out=v, in_=v, compare_op=ALU.not_equal, fill=SCALING, base=0,
                               pattern=[[-P // RANK, ZC], [-1, P // RANK], [0, RANK]],
                               channel_multiplier=1).then_inc(expand_ready, 1)
            pool.wait_ge(expand_ready, 2)
            for a in range(ZC):
                pool.wait_ge(z_hi_done, a + 1)
                pool.tensor_tensor(z_lo[:, a, :], z[:, a % 2, :], z_hi[:, a, :].bitcast(F32),
                                   ALU.subtract).then_inc(z_lo_done, 1)

        @block.scalar
        def _(act):
            def item_hi(m, q):
                n = t_item(m, q)
                act.wait_ge(t_done, n + 1)
                act.activation(w_hi[:, m % 2, q * 512:(q + 1) * 512], ps_t[:, n % 3, :], ACT.Copy).then_inc(hi_done, 1)

            def z_high(a):
                act.wait_ge(z_gated, a + 1)
                act.activation(z_hi[:, a, :], z[:, a % 2, :], ACT.Copy).then_inc(z_hi_done, 1)

            for n in range(NORM_T):
                act.wait_ge(t_done, n + 1)
                act.activation(h_slot(h_hi, n), quad(ps_t, n % 3), ACT.Copy).then_inc(hi_done, 1)
            for q in range(4):
                item_hi(0, q)
            act.wait_ge(t_done, T_WQ + 1)
            act.wait_ge(wq_zero, 1)
            bank = T_WQ % 3
            act.activation(wq_t[:, :, 0:RD], ps_t[:, bank, 0:DC * RD].rearrange("p (c r) -> p c r", r=RD),
                           ACT.Copy).then_inc(hi_done, 1)
            act.activation(keys_t[:], ps_t[0:RD, bank, DC * RD:DC * RD + EXPERTS], ACT.Copy).then_inc(keys_out, 1)
            act.wait_ge(q_done, 1)
            act.activation(q_half, ps_r[WQ_LO:WQ_LO + RD, 0, :], ACT.Copy).then_inc(q_half_out, 1)
            item_hi(1, 0)
            item_hi(1, 1)
            act.wait_ge(sc_shifted, 1)
            act.activation(expo[:], shifted[:], ACT.Exp).then_inc(exp_done, 1)
            item_hi(1, 2)
            item_hi(1, 3)
            act.wait_ge(gt_done, 1)
            act.activation(gate_t[:], ps_r[0:EXPERTS, 2, :], ACT.Copy).then_inc(gt_out, 1)
            item_hi(2, 0)
            for a in range(ZC):
                act.wait_ge(gx_done, a + 1)
                act.activation(gates[:, a, :], ps_r[:, a % 2, :], ACT.Copy).then_inc(gx_out, 1)
            z_high(0)
            for q in range(1, 4):
                item_hi(2, q)
            z_high(1)
            for m in range(3, ITEMS):
                for q in range(4):
                    item_hi(m, q)
                if m - 1 < ZC:
                    z_high(m - 1)

        @block.vector
        def _(dve):
            links = [0]

            def link(ins):
                ins.then_inc(chain, 1)
                links[0] += 1
                dve.wait_ge(chain, links[0])

            def norm_lo(n):
                dve.wait_ge(hi_done, n + 1)
                dve.tensor_tensor(h_slot(h_lo, n), quad(ps_t, n % 3), h_slot(h_hi, n).bitcast(F32),
                                  ALU.subtract).then_inc(lo_done, 1)

            def free_or_evacuate(r):
                if r >= 2:
                    for n in range((r - 2) * QUADS, (r - 1) * QUADS):
                        norm_lo(n)
                    dve.wait_ge(t_done, QUADS * (r - 1))

            def item_lo(m, q):
                n = t_item(m, q)
                dve.wait_ge(hi_done, n + 1)
                part = slice(q * 512, (q + 1) * 512)
                dve.tensor_tensor(w_lo[:, m % 2, part], ps_t[:, n % 3, :], w_hi[:, m % 2, part].bitcast(F32),
                                  ALU.subtract).then_inc(lo_done, 1)

            def gate_z(a):
                dve.wait_ge(z_done, a + 1)
                dve.wait_ge(gx_out, a + 1)
                if a >= 2:
                    dve.wait_ge(z_lo_done, a - 1)
                dve.tensor_tensor(z[:, a % 2, :], ps_mm[:, a % 2, :], gates[:, a, :], ALU.mult).then_inc(z_gated, 1)

            rows_norm_vector(dve, link, rows, row_bn, mv, rs_w, normed, norm_ready, free_or_evacuate)
            for n in range(2 * QUADS, NORM_T):
                norm_lo(n)
            for q in range(4):
                item_lo(0, q)
            dve.wait_ge(hi_done, T_WQ + 1)
            dve.wait_ge(keys_out, 1)
            dve.tensor_tensor(wq_t[:, :, WQ_LO:WQ_LO + RD],
                              ps_t[:, T_WQ % 3, 0:DC * RD].rearrange("p (c r) -> p c r", r=RD),
                              wq_t[:, :, 0:RD].bitcast(F32), ALU.subtract).then_inc(lo_done, 1)

            dve.wait_ge(q_half_out, 1)
            dve.tensor_tensor(q_t, ps_r[0:RD, 0, :], q_half, ALU.add).then_inc(q_ready, 1)
            dve.wait_ge(sc_done, 1)
            link(dve.tensor_copy(sc[:], ps_r[:, 1, 0:RT * EXPERTS].rearrange("p (r e) -> p r e", r=RT)))
            for r in range(RT):
                i = dve.max(best[:, r, 0:8], sc[:, r, :])
            link(i)
            dve.tensor_tensor(shifted[:], sc[:], best[:, :, 0:1].to_broadcast([P, RT, EXPERTS]),
                              ALU.subtract).then_inc(sc_shifted, 1)
            item_lo(1, 0)
            for r in range(RT):
                i = dve.match_replace(out=rest[:, 0, r, :], in_to_replace=best[:, r, 0:8], in_values=sc[:, r, :],
                                      imm_value=-3.0e38)
            link(i)
            for r in range(RT):
                i = dve.max(best[:, r, 8:16], rest[:, 0, r, :])
            link(i)
            item_lo(1, 1)
            for r in range(RT):
                i = dve.match_replace(out=rest[:, 1, r, :], in_to_replace=best[:, r, 8:16], in_values=rest[:, 0, r, :],
                                      imm_value=-3.0e38)
            link(i)
            link(dve.tensor_tensor(chosen[:], rest[:, 1, :, :], sc[:], ALU.not_equal))
            dve.wait_ge(exp_done, 1)
            link(dve.tensor_tensor(chosen[:], chosen[:], expo[:], ALU.mult))
            link(dve.tensor_reduce(g_sum[:], chosen[:], AX.X, ALU.add))
            link(dve.reciprocal(g_inv[:], g_sum[:]))
            dve.tensor_tensor(gate[:], chosen[:], g_inv[:].unsqueeze(2).to_broadcast([P, RT, EXPERTS]),
                              ALU.mult).then_inc(gate_ready, 1)
            item_lo(1, 2)
            item_lo(1, 3)
            item_lo(2, 0)
            gate_z(0)
            for q in range(1, 4):
                item_lo(2, q)
            gate_z(1)
            for m in range(3, ZC + 1):
                for q in range(4):
                    item_lo(m, q)
                gate_z(m - 1)
            for c in range(NCOL):
                for r in range(RT):
                    n = RT * c + r
                    dve.wait_ge(o_done, n + 1)
                    part = rows[:, r, c * 512:(c + 1) * 512]
                    dve.tensor_tensor(part, part, ps_mm[:, n % 2, :], ALU.add).then_inc(o_added, 1)
                    if ZC + c + 1 < ITEMS:
                        item_lo(ZC + c + 1, r)

        @block.tensor
        def _(pe):
            def t_wait(n):
                if n >= 3:
                    pe.wait_ge(lo_done, n - 2)

            def transpose_item(m, q):
                n = t_item(m, q)
                t_wait(n)
                if q == 0:
                    pe.wait_ge(raw_in[m % 2], 16 * (m // 2 + 1))
                for c in range(4):
                    at = (4 * q + c) * P if m < ZC else c * 512 + q * P
                    i = pe.transpose(ps_t[:, n % 3, c * P:(c + 1) * P], raw[:, m % 2, at:at + P], ident[:])
                i.then_inc(t_done, 1)

            for n in range(NORM_T):
                if n % QUADS == 0:
                    pe.wait_ge(norm_ready, n // QUADS + 1)
                t_wait(n)
                rows_transpose_slot(pe, n, normed, ident, ps_t, n % 3).then_inc(t_done, 1)
            for q in range(4):
                transpose_item(0, q)
            t_wait(T_WQ)
            pe.wait_ge(small_in, 32)
            bank = T_WQ % 3
            for c in range(DC):
                pe.transpose(ps_t[:, bank, c * RD:(c + 1) * RD], wq_sb[:, c * P:(c + 1) * P], ident[0:RD, 0:RD])
            pe.transpose(ps_t[0:RD, bank, DC * RD:DC * RD + EXPERTS], keys_sb[:],
                         ident[0:EXPERTS, 0:EXPERTS]).then_inc(t_done, 1)
            pe.wait_ge(lo_done, T_WQ + 1)
            for c in range(DC):
                pe.matmul(ps_r[:, 0, :], wq_t[:, c, :], h_hi[:, c, :], start=c == 0, stop=False)
                i = pe.matmul(ps_r[:, 0, :], wq_t[:, c, :], h_lo[:, c, :], start=False, stop=c == DC - 1)
            i.then_inc(q_done, 1)

            def router_scores():
                pe.wait_ge(q_ready, 1)
                pe.wait_ge(keys_out, 1)
                for r in range(RT):
                    i = pe.matmul(ps_r[:, 1, r * EXPERTS:(r + 1) * EXPERTS], q_t[:, r * P:(r + 1) * P], keys_t[:],
                                  start=True, stop=True)
                i.then_inc(sc_done, 1)

            def gate_transpose():
                pe.wait_ge(gate_ready, 1)
                for r in range(RT):
                    i = pe.transpose(ps_r[0:EXPERTS, 2, r * P:(r + 1) * P], gate[:, r, :], ident[:])
                i.then_inc(gt_done, 1)

            def expand_gates():
                pe.wait_ge(expand_ready, 2)
                pe.wait_ge(gt_out, 1)
                for a in range(ZC):
                    if a >= 2:
                        pe.wait_ge(gx_out, a - 1)
                    pe.matmul(ps_r[:, a % 2, :], expand[:, a, :], gate_t[:], start=True, stop=True).then_inc(gx_done, 1)

            def down(a):
                if a >= 2:
                    pe.wait_ge(z_gated, a - 1)
                pe.wait_ge(lo_done, t_item(a, 3) + 1)
                for q in range(4):
                    for c in range(4 * q, 4 * q + 4):
                        col = slice(c * P, (c + 1) * P)
                        i = three_products(pe, ps_mm[:, a % 2, :], w_hi[:, a % 2, col], w_lo[:, a % 2, col],
                                           h_hi[:, c, :], h_lo[:, c, :], c == 0, c == DC - 1)
                    if a == 0 and q == 0:
                        router_scores()
                    if q < 3:
                        transpose_item(a + 1, q)
                    if a == 1 and q == 0:
                        expand_gates()
                i.then_inc(z_done, 1)
                if a == 0:
                    gate_transpose()
                transpose_item(a + 1, 3)

            def up(c):
                m = ZC + c
                pe.wait_ge(lo_done, t_item(m, 3) + 1)
                for r in range(RT):
                    n = RT * c + r
                    if n >= 2:
                        pe.wait_ge(o_added, n - 1)
                    for a in range(ZC):
                        if c == 0 and r == 0:
                            pe.wait_ge(z_lo_done, a + 1)
                        col = slice(r * P, (r + 1) * P)
                        wc = slice(a * 512, (a + 1) * 512)
                        i = three_products(pe, ps_mm[:, n % 2, :], z_hi[:, a, col], z_lo[:, a, col],
                                           w_hi[:, m % 2, wc], w_lo[:, m % 2, wc], a == 0, a == ZC - 1)
                    i.then_inc(o_done, 1)
                    if m + 1 < ITEMS:
                        transpose_item(m + 1, r)

            for a in range(ZC):
                down(a)
            pe.wait_ge(z_gated, ZC)
            for c in range(NCOL):
                up(c)


_INS = ['x', 'ctx_4096', 'L0_attn_w_q', 'L0_attn_w_k', 'L0_attn_w_v', 'L0_attn_w_o', 'L0_ffn_A_w', 'L0_ffn_B_w',
        'L0_ffn_Wq_w', 'L0_ffn_keys']


def kernel(**inputs):
    import numpy as _np
    import concourse.bacc as _bacc
    from concourse.bass_utils import run_bass_kernel_spmd as _run

    nc = _bacc.Bacc("TRN2", target_bir_lowering=False, num_devices=1)
    arrays, args = {}, []
    for name in _INS:
        a = _np.ascontiguousarray(inputs[name])
        arrays[f"in_{name}"] = a
        args.append(nc.dram_tensor(f"in_{name}", a.shape, mybir.dt.from_np(a.dtype), kind="ExternalInput").ap())
    args.append(nc.dram_tensor("out_x", (B, LQ, D), F32, kind="ExternalOutput").ap())
    kernel_program(nc, *args)
    r = _run(nc, [arrays], core_ids=[0])
    return r.results[0]["out_x"]
```
